# Optimizing a Trainium2 kernel written in Bass

```python
import numpy as np
import jax
import jax.numpy as jnp

def _softmax(x, axis=-1):
    return jax.nn.softmax(x, axis=axis)
def _gelu(x):
    return jax.nn.gelu(x, approximate=True)
def _silu(x):
    return jax.nn.silu(x)
def _sigmoid(x):
    return jax.nn.sigmoid(x)
def _layernorm(x, axis=-1, eps=1e-5):
    m = jnp.mean(x, axis=axis, keepdims=True)
    v = jnp.var(x, axis=axis, keepdims=True)
    return (x - m) / jnp.sqrt(v + eps)
def _scatter_add(tgt, idx, src, axis=0):
    return tgt.at[idx].add(src)
def _segment_sum(src, seg, n):
    return jax.ops.segment_sum(src, seg, n)

kernel_name = 'mk_conv_seq_d1_conv_nchw512_fe39cf'

def setup_inputs(seed: int = 0):
    np.random.seed(seed)
    _w = jnp.asarray
    def _rec_inputs():
        import jax
        import jax.numpy as jnp
        _gk = jax.random.key(seed)
        x = 7.22e-05 + 1 * jax.random.normal(jax.random.fold_in(_gk, 1), (16, 512, 32, 32), jnp.float32)
        return x
    x = _rec_inputs()
    def _L0_conv_setup():
        import jax, jax.numpy as jnp
        import numpy as np
        NUM_HEADS = 8
        NUM_GROUPS = 32
        EPS = 1e-05

        def group_norm(x, gamma, beta):
            b, c, h, w = x.shape
            xg = x.reshape(b, NUM_GROUPS, c // NUM_GROUPS, h, w)
            mean = jnp.mean(xg, axis=(2, 3, 4), keepdims=True)
            var = jnp.var(xg, axis=(2, 3, 4), keepdims=True)
            xn = ((xg - mean) * jax.lax.rsqrt(var + EPS)).reshape(b, c, h, w)
            return xn * gamma[None, :, None, None] + beta[None, :, None, None]
        key = jax.random.key(seed)
        ks = jax.random.split(key, 4)
        b, c, h, w = (16, 512, 32, 32)
        x = jax.random.normal(ks[0], (b, c, h, w), dtype=jnp.float32)
        gn_gamma = jnp.ones((c,), dtype=jnp.float32)
        gn_beta = jnp.zeros((c,), dtype=jnp.float32)
        qkv_w = jax.random.normal(ks[1], (3 * c, c), dtype=jnp.float32) * (1.0 / np.sqrt(c))
        qkv_b = jnp.zeros((3 * c,), dtype=jnp.float32)
        proj_w = jax.random.normal(ks[2], (c, c), dtype=jnp.float32) * (1.0 / np.sqrt(c))
        proj_b = jnp.zeros((c,), dtype=jnp.float32)
        return {'x': x, 'gn_gamma': gn_gamma, 'gn_beta': gn_beta, 'qkv_w': qkv_w, 'qkv_b': qkv_b, 'proj_w': proj_w, 'proj_b': proj_b}
    _L0_conv_all = _L0_conv_setup()
    _L0_conv_in = {k: v for k, v in _L0_conv_all.items() if k in ('gn_gamma', 'gn_beta', 'qkv_w', 'qkv_b', 'proj_w', 'proj_b', )}
    del _L0_conv_all

    return {
        "x": x,
        "L0_conv_gn_gamma": _L0_conv_in["gn_gamma"],
        "L0_conv_gn_beta": _L0_conv_in["gn_beta"],
        "L0_conv_qkv_w": _L0_conv_in["qkv_w"],
        "L0_conv_qkv_b": _L0_conv_in["qkv_b"],
        "L0_conv_proj_w": _L0_conv_in["proj_w"],
        "L0_conv_proj_b": _L0_conv_in["proj_b"],
    }

def reference(x, L0_conv_gn_gamma, L0_conv_gn_beta, L0_conv_qkv_w, L0_conv_qkv_b, L0_conv_proj_w, L0_conv_proj_b):
    import jax
    import jax.numpy as jnp
    def _L0_conv_ref(x, gn_gamma, gn_beta, qkv_w, qkv_b, proj_w, proj_b):
        import jax, jax.numpy as jnp
        import numpy as np
        NUM_HEADS = 8
        NUM_GROUPS = 32
        EPS = 1e-05

        def group_norm(x, gamma, beta):
            b, c, h, w = x.shape
            xg = x.reshape(b, NUM_GROUPS, c // NUM_GROUPS, h, w)
            mean = jnp.mean(xg, axis=(2, 3, 4), keepdims=True)
            var = jnp.var(xg, axis=(2, 3, 4), keepdims=True)
            xn = ((xg - mean) * jax.lax.rsqrt(var + EPS)).reshape(b, c, h, w)
            return xn * gamma[None, :, None, None] + beta[None, :, None, None]
        b, c, h, w = x.shape
        hd = c // NUM_HEADS
        hw = h * w
        xn = group_norm(x, gn_gamma, gn_beta)
        qkv = jnp.einsum('oc,bchw->bohw', qkv_w, xn) + qkv_b[None, :, None, None]
        q, k, v = jnp.split(qkv, 3, axis=1)
        q = q.reshape(b, NUM_HEADS, hd, hw)
        k = k.reshape(b, NUM_HEADS, hd, hw)
        v = v.reshape(b, NUM_HEADS, hd, hw)
        scale = 1.0 / np.sqrt(hd)
        attn = jnp.einsum('bhdt,bhds->bhts', q, k) * scale
        attn = jax.nn.softmax(attn, axis=-1)
        h_attn = jnp.einsum('bhts,bhds->bhdt', attn, v).reshape(b, c, h, w)
        h_attn = jnp.einsum('oc,bchw->bohw', proj_w, h_attn) + proj_b[None, :, None, None]
        return x + h_attn

    def _gn(v, G=32, eps=1e-5):
        B_, C_, H_, W_ = v.shape
        g = v.reshape(B_, G, C_ // G, H_, W_)
        m = jnp.mean(g, axis=(2, 3, 4), keepdims=True)
        s = jnp.var(g, axis=(2, 3, 4), keepdims=True)
        return ((g - m) / jnp.sqrt(s + eps)).reshape(v.shape)

    def _ln_c(v, eps=1e-6):
        m = jnp.mean(v, axis=1, keepdims=True)
        s = jnp.var(v, axis=1, keepdims=True)
        return (v - m) / jnp.sqrt(s + eps)

    def _ln_t(v, eps=1e-5):
        m = jnp.mean(v, axis=-1, keepdims=True)
        s = jnp.var(v, axis=-1, keepdims=True)
        return (v - m) / jnp.sqrt(s + eps)

    def _to_tokens(v):
        B_, C_, H_, W_ = v.shape
        return v.reshape(B_, C_, H_ * W_).transpose(0, 2, 1)
    def _from_tokens(t, like):
        B_, C_, H_, W_ = like.shape
        return t.transpose(0, 2, 1).reshape(B_, C_, H_, W_)

    x = _L0_conv_ref(x, L0_conv_gn_gamma, L0_conv_gn_beta, L0_conv_qkv_w, L0_conv_qkv_b, L0_conv_proj_w, L0_conv_proj_b)
    return x


_drawn_inputs = setup_inputs


def setup_inputs(seed=0):
    import zlib

    import numpy as np

    out = dict(_drawn_inputs(seed))
    spreads = {'L0_conv_gn_gamma': (1.0, 0.544),
     'L0_conv_gn_beta': (0.0, 0.1),
     'L0_conv_qkv_b': (0.0, 0.1),
     'L0_conv_proj_b': (0.0, 0.1)}
    factors = {}
    for name, (base, spread) in spreads.items():
        noise = np.random.default_rng([zlib.crc32(name.encode()), seed]).standard_normal(out[name].shape)
        drawn = base * np.exp(spread * noise) if base else spread * noise
        out[name] = jnp.asarray(drawn.astype(out[name].dtype))
    for name, factor in factors.items():
        out[name] = (out[name] * factor).astype(out[name].dtype)
    return out
```

```python
from contextlib import ExitStack

import concourse.bass as bass
from concourse import mybir

F32 = mybir.dt.float32
F32R = mybir.dt.float32r
F16 = mybir.dt.float16
U32 = mybir.dt.uint32
I32 = mybir.dt.int32
ALU = mybir.AluOpType
ACT = mybir.ActivationFunctionType
AX = mybir.AxisListType

P = 128
HEADS = 8
GROUPS = 32
EPS = 1e-5
X_SCALE = 2.0 ** 8
W_TOP = 2.0 ** 14
V_SCALE = 2.0 ** -15
P_SCALE = 2.0 ** 15


def attention_block(nc, x, gamma, beta, qkv_w, qkv_b, proj_w, proj_b, out):
    B, C, HGT, WID = x.shape
    T = HGT * WID
    CB = C // P
    HD = C // HEADS
    PAIRS = HEADS // 2
    HALF = T // 2
    QT = T // 4
    ST = T // P
    WT_TILES = 4 * CB
    STEPS = HEADS * ST
    UNITS = STEPS // 4
    PRE = 8
    NCH = 32
    STAT = 43
    GROUP_IN, GROUP_OUT, X_HIGH = 15, 16, 37
    SCALE_Q = float(HD) ** -0.5
    assert T == 1024 and C == 512 and HD == 64 and SCALE_Q == 0.125

    xv = x.rearrange("b (c p) h w -> b p c (h w)", p=P)
    ov = out.rearrange("b (c p) h w -> b p c (h w)", p=P)

    with ExitStack() as ctx:
        def sb(name, shape, dt):
            return ctx.enter_context(nc.sbuf_tensor(name, shape, dt))

        def sem(name):
            return ctx.enter_context(nc.semaphore(name))

        wt_hi = sb("wt_hi", [P, CB, WT_TILES * P], F16)
        wt_lo = sb("wt_lo", [P, CB, WT_TILES * P], F16)
        pt_hi = sb("pt_hi", [P, 2, 2, ST, QT], F16)
        pt_lo = sb("pt_lo", [P, 2, 2, ST, QT], F16)
        xn_hi = sb("xn_hi", [P, CB, T], F16)
        xn_lo = sb("xn_lo", [P, CB, T], F16)
        xs = sb("xs", [P, CB, T], F32)
        q0 = sb("q0", [P, 2, HALF], F32R)
        q1 = sb("q1", [P, 2, 2, HALF], F32R)
        k_hi = sb("k_hi", [P, 2, 2, T], F32R)
        k_lo = sb("k_lo", [P, 2, 2, T], F32R)
        v_hi = sb("v_hi", [P, ST, C], F16)
        v_lo = sb("v_lo", [P, ST, C], F16)
        prob = sb("prob", [P, 2, T], F32)
        on_hi = sb("on_hi", [P, 2 * CB * T], F16)
        on_lo = sb("on_lo", [P, 2 * CB * T], F16)
        fl = sb("fl", [P, 2, HALF], F32)
        hs = sb("hs", [P, 2, HALF], F32)
        onorm = sb("onorm", [P, QT], F32)
        rb = sb("rb", [P, 2, 2, HD], F32)
        ident = sb("ident", [P, P], F32)
        grp = sb("grp", [P, P], F32)
        inv = sb("inv", [P, WT_TILES], F32)
        bias = sb("bias", [P, WT_TILES], F32)
        small = sb("small", [P, 64], F32)
        xstat = sb("xstat", [P, 96], F32)
        sums = sb("sums", [P, 2, 4], F32)
        rcp = sb("rcp", [P, 4], F32)
        nmax = sb("nmax", [P, 2], F32)

        scores = ctx.enter_context(nc.psum_tensor("scores", [P, 2, T], F32))
        tr = ctx.enter_context(nc.psum_tensor("tr", [P, 2, 4, P], F32))
        acc = ctx.enter_context(nc.psum_tensor("acc", [P, 2, QT], F32))
        mix = ctx.enter_context(nc.psum_tensor("mix", [P, HALF], F32))

        s_w_in = [sem("s_w_in0"), sem("s_w_in1")]
        s_par_in = sem("s_par_in")
        s_const = sem("s_const")
        s_setup = sem("s_setup")
        s_wtr = sem("s_wtr")
        s_wh = sem("s_wh")
        s_wl = sem("s_wl")
        s_rowb = sem("s_rowb")
        s_x_in = sem("s_x_in")
        s_stat = sem("s_stat")
        s_gsum = sem("s_gsum")
        s_xlo = sem("s_xlo")
        s_scores = sem("s_scores")
        s_max = sem("s_max")
        s_exp = sem("s_exp")
        s_tr = sem("s_tr")
        s_phi = sem("s_phi")
        s_plo = sem("s_plo")
        s_pv = sem("s_pv")
        s_rcp = sem("s_rcp")
        s_rb = sem("s_rb")
        s_rt = sem("s_rt")
        s_rs = sem("s_rs")
        s_norm = sem("s_norm")
        s_onh = sem("s_onh")
        s_on = sem("s_on")
        s_held = sem("s_held")
        s_chunk = sem("s_chunk")
        s_ev = sem("s_ev")
        s_qkh = sem("s_qkh")
        s_vh = sem("s_vh")
        s_split = sem("s_split")
        s_stk = [sem("s_stk0"), sem("s_stk1")]
        s_res = [sem("s_res0"), sem("s_res1")]
        s_out = [sem("s_out0"), sem("s_out1")]

        QK, V, PROJ = "qk", "v", "proj"
        KINDS = [("k", 0), ("k", 1), ("q", 1), ("q", 0)]

        def slot(b, m):
            w, j = divmod(m, 8)
            if j < 4:
                return (QK, int(w == 3), ((w + 1) % PAIRS, j))
            if w in (0, 3):
                return (V, int(w == 3), (int(w == 0), j - 4))
            return (PROJ, -1, (w - 1) * 4 + j - 4)

        def active(b, m):
            kind, db, _ = slot(b, m)
            if isinstance(b, int):
                return 0 <= b + db < B
            return True

        def number(b, m):
            if isinstance(b, int) and b == 0:
                return PRE + sum(active(0, j) for j in range(m))
            return NCH * b + m

        def qk_number(b, m):
            _, db, (p, j) = slot(b, m)
            return (b + db) * 4 * PAIRS + 4 * p + j

        def v_number(b, m):
            _, db, (g, j) = slot(b, m)
            return (b + db) * 8 + 4 * g + j

        def stacked(pair, j):
            return pair * 192 + (128 if j < 2 else 192)

        def parity(b):
            return b % 2

        def tiles_of(kind, what):
            if kind == QK:
                p, j = what
                return (4 + p) if KINDS[j][0] == "k" else p
            return 8 if kind == V else 12 + what % 4

        def weight_bank(t):
            bank = scores[:, (t // 2) % 2, (t % 2) * HALF:(t % 2 + 1) * HALF]
            return bank.rearrange("p (c o) -> p c o", c=CB)

        def hold(engine):
            engine.sem_inc(s_held, 1)

        PRE_CHUNKS = [(QK, (0, j)) for j in range(4)] + [(V, (0, j)) for j in range(4)]

        block = ctx.enter_context(nc.Block())

        setup_at = {}

        @block.vector
        def _(dve):
            def low_weights(t):
                dve.wait_ge(s_wh, t + 1)
                cols = slice(t * P, (t + 1) * P)
                dve.tensor_tensor(wt_lo[:, :, cols], weight_bank(t), wt_hi[:, :, cols],
                                  ALU.subtract).then_inc(s_wl, 1)

            count = [0]

            def mark(ins):
                ins.then_inc(s_setup, 1)
                count[0] += 1
                return count[0]

            def settle():
                dve.wait_ge(s_setup, count[0])

            tot, pw, rc = small[:, 0:16], small[:, 16:32], small[:, 32:48]
            dve.wait_ge(s_par_in, 64)
            dve.wait_ge(s_const, 6)
            for t in range(WT_TILES):
                wn, wm, junk = hs[:, t % 2, :], prob[:, 1, (t % 2) * C:(t % 2 + 1) * C], onorm[:]
                if t == 12:
                    settle()
                    mark(dve.tensor_scalar(small[:, 48:52], pw[:, 8:12], 1.0 / (W_TOP * X_SCALE * V_SCALE),
                                           None, ALU.mult))
                    settle()
                    for i in range(4):
                        mark(dve.tensor_scalar(prob[:, 0, i * P:(i + 1) * P], ident[:], 0.0,
                                               small[:, 48 + i:49 + i], ALU.mult, ALU.add))
                        mark(dve.tensor_scalar(prob[:, 0, (4 + i) * P:(5 + i) * P], ident[:], 0.0,
                                               bias[:, 8 + i:9 + i], ALU.mult, ALU.add))
                    setup_at["spread"] = count[0]
                    dve.wait_ge(s_rowb, 1)
                mul_row = fl[:, 0, :] if t < 12 else mix[:]
                add_row = fl[:, 1, :] if t < 12 else acc[:].rearrange("p a b -> p (a b)")
                dve.wait_ge(s_w_in[t % 2], 16 * (t // 2 + 1))
                if t >= 2:
                    dve.wait_ge(s_wtr, t - 1)
                    settle()
                mark(dve.tensor_tensor(wm, wn, mul_row, ALU.mult))
                for h in range(2):
                    cols = slice(h * QT, (h + 1) * QT)
                    settle()
                    mark(dve.tensor_tensor_reduce(out=junk, in0=wn[:, cols], in1=add_row[:, cols], scale=1.0,
                                                  scalar=0.0, op0=ALU.mult, op1=ALU.add,
                                                  accum_out=small[:, 60 + h:61 + h]))
                setup_at["wn_free", t] = count[0]
                settle()
                mark(dve.scalar_tensor_tensor(out=small[:, 62:63], in0=small[:, 60:61], scalar=1.0,
                                              in1=small[:, 61:62], op0=ALU.mult, op1=ALU.add))
                mark(dve.tensor_reduce(tot[:, t:t + 1], wm, AX.X, ALU.add, apply_absolute_value=True))
                settle()
                mark(dve.tensor_tensor(bias[:, t:t + 1], bias[:, t:t + 1], small[:, 62:63], ALU.add))
                mark(dve.tensor_scalar(small[:, 63:64], tot[:, t:t + 1], 2.0 ** -100, None, ALU.max))
                settle()
                mark(dve.tensor_scalar(pw[:, t:t + 1].bitcast(U32), small[:, 63:64].bitcast(U32), 0x7F800000, None,
                                       ALU.bitwise_and))
                settle()
                mark(dve.reciprocal(rc[:, t:t + 1], pw[:, t:t + 1]))
                settle()
                setup_at["wm", t] = mark(dve.tensor_scalar(wm, wm, rc[:, t:t + 1], W_TOP, ALU.mult, ALU.mult))
                if t >= 1:
                    low_weights(t - 1)
            low_weights(WT_TILES - 1)
            settle()
            mark(dve.tensor_scalar(inv[:, 0:4], pw[:, 0:4], SCALE_Q / (W_TOP * X_SCALE), None, ALU.mult))
            mark(dve.tensor_scalar(inv[:, 4:8], pw[:, 4:8], 1.0 / (W_TOP * X_SCALE), None, ALU.mult))
            mark(dve.tensor_scalar(inv[:, 12:16], pw[:, 12:16], 1.0 / W_TOP, None, ALU.mult))
            mark(dve.tensor_scalar(bias[:, 0:4], bias[:, 0:4], SCALE_Q, None, ALU.mult))
            mark(dve.memset(bias[:, 8:12], 0.0))
            settle()
            setup_at["done"] = count[0]

            bns = xstat[:, 0:48].rearrange("p (n s) -> p n s", s=6)
            mv = xstat[:, 48:56].rearrange("p (c s) -> p c s", s=2)
            gin, gout = xstat[:, 56:64], xstat[:, 64:72]
            t1, var, t3, y, a_x, b_x = [xstat[:, 72 + 4 * i:76 + 4 * i] for i in range(6)]

            class Norm:
                def __init__(self, b):
                    self.b, self.base, self.n = b, STAT * b, 0

                def mark(self, ins):
                    ins.then_inc(s_stat, 1)
                    self.n += 1

                def settle(self):
                    dve.wait_ge(s_stat, self.base + self.n)

                def stats(self, c):
                    if c == 0:
                        dve.wait_ge(s_x_in, 16 * (self.b + 1))
                    for h in range(2):
                        self.mark(dve.bn_stats(bns[:, 2 * c + h, :], xs[:, c, h * HALF:(h + 1) * HALF]))

                def channel_means(self):
                    self.settle()
                    hold(dve)
                    for c in range(CB):
                        self.mark(dve.bn_aggr(mv[:, c, :], bns[:, 2 * c:2 * c + 2, :]))
                    self.settle()
                    self.mark(dve.tensor_tensor(t1, mv[:, :, 0], mv[:, :, 0], ALU.mult))
                    self.settle()
                    self.mark(dve.tensor_tensor(gin[:, 4:8], t1, mv[:, :, 1], ALU.add))
                    self.mark(dve.tensor_copy(gin[:, 0:4], mv[:, :, 0]))
                    assert self.n == GROUP_IN

                def group_out(self):
                    dve.wait_ge(s_gsum, self.b + 1)
                    self.mark(dve.tensor_copy(gout, mix[:, 0:8]))
                    assert self.n == GROUP_OUT

                def factors(self):
                    mean = gout[:, 0:4]
                    self.settle()
                    self.mark(dve.tensor_tensor(t1, mean, mean, ALU.mult))
                    self.settle()
                    self.mark(dve.tensor_tensor(var, gout[:, 4:8], t1, ALU.subtract))
                    self.settle()
                    self.mark(dve.tensor_scalar(var, var, 0.0, EPS, ALU.max, ALU.add))
                    self.settle()
                    self.mark(dve.tensor_scalar(t1.bitcast(U32), var.bitcast(U32), 1, None, ALU.logical_shift_right))
                    self.settle()
                    self.mark(dve.tensor_scalar(y.bitcast(I32), t1.bitcast(I32), -1.0, float(0x5F3759DF),
                                                ALU.mult, ALU.add))
                    for _ in range(3):
                        self.settle()
                        self.mark(dve.tensor_tensor(t1, y, y, ALU.mult))
                        self.settle()
                        self.mark(dve.tensor_tensor(t3, t1, var, ALU.mult))
                        self.settle()
                        self.mark(dve.tensor_scalar(t1, t3, -0.5, 1.5, ALU.mult, ALU.add))
                        self.settle()
                        self.mark(dve.tensor_tensor(y, y, t1, ALU.mult))
                    self.settle()
                    self.mark(dve.tensor_scalar(a_x, y, X_SCALE, None, ALU.mult))
                    self.settle()
                    self.mark(dve.scalar_tensor_tensor(out=b_x, in0=mean, scalar=-1.0, in1=a_x,
                                                       op0=ALU.mult, op1=ALU.mult))

                def apply(self, c):
                    self.settle()
                    self.mark(dve.tensor_scalar(xs[:, c, :], xs[:, c, :], a_x[:, c:c + 1], b_x[:, c:c + 1],
                                                ALU.mult, ALU.add))
                    self.settle()
                    self.mark(dve.tensor_copy(xn_hi[:, c, :], xs[:, c, :]))
                    assert self.n == X_HIGH + 2 * c

            n0 = Norm(0)
            for c in range(CB):
                n0.stats(c)
            n0.channel_means()
            n0.group_out()
            n0.factors()
            for c in range(CB):
                n0.apply(c)
            assert n0.n == STAT

            def row_max(K, buf):
                dve.wait_ge(s_scores, K + 1)
                dve.tensor_reduce(nmax[:, buf:buf + 1], scores[:, buf, :], AX.X, ALU.max,
                                  negate=True).then_inc(s_max, 1)

            def low(K, buf, head, tt, half, ubuf):
                dve.wait_ge(s_phi, 2 * K + half + 1)
                at = (slice(None), ubuf, head, slice(4 * half, 4 * half + 4), slice(tt * P, (tt + 1) * P))
                dve.scalar_tensor_tensor(out=pt_lo[at], in0=tr[:, half], scalar=P_SCALE, in1=pt_hi[at],
                                         op0=ALU.mult, op1=ALU.subtract).then_inc(s_plo, 1)

            def reciprocals(unit, ubuf, again):
                dve.wait_ge(s_exp, 4 * unit + 4)
                if again:
                    dve.wait_ge(s_rt, unit)
                dve.reciprocal(rcp[:], sums[:, ubuf, :]).then_inc(s_rcp, 1)
                dve.wait_ge(s_rcp, unit + 1)
                for head in range(2):
                    for tt in range(2):
                        col = rcp[:, 2 * head + tt:2 * head + tt + 1]
                        ins = dve.tensor_scalar(rb[:, tt, head, :], ident[:, 0:HD], 0.0, col, ALU.mult, ALU.add)
                ins.then_inc(s_rb, 1)

            def normalise(unit, again):
                dve.wait_ge(s_rt, unit + 1)
                if again:
                    dve.wait_ge(s_on, unit)
                dve.tensor_copy(onorm[:], acc[:, 1, :]).then_inc(s_rs, 1)
                dve.wait_ge(s_rs, unit + 1)
                dve.scalar_tensor_tensor(out=onorm[:], in0=acc[:, 0, :], scalar=1.0 / P_SCALE, in1=onorm[:],
                                         op0=ALU.mult, op1=ALU.mult).then_inc(s_norm, 1)

            row_max(0, 0)
            row_max(1, 1)

            def batch(b):
                first, last = isinstance(b, int) and b == 0, isinstance(b, int) and b == B - 1
                norm = None if last else Norm(b + 1)
                for k in range(STEPS):
                    K, u, i = STEPS * b + k, k // 4, k % 4
                    if i == 0 and not (first and u == 0):
                        reciprocals(UNITS * b + u - 1, (u - 1) % 2, not (first and u == 1))
                    if i == 0 and not (first and u < 2):
                        normalise(UNITS * b + u - 2, not (first and u == 2))
                    if not (last and k >= STEPS - 2):
                        row_max(K + 2, k % 2)
                    for half in range(2):
                        low(K, k % 2, i // 2, i % 2, half, u % 2)
                    if norm:
                        if 32 <= k < 36:
                            norm.stats(k - 32)
                        if k == 36:
                            norm.channel_means()
                        if k == 40:
                            norm.group_out()
                            norm.factors()
                        if 42 <= k < 46:
                            norm.apply(k - 42)
                if norm:
                    assert norm.n == STAT

            batch(0)
            with dve.Fori(1, B - 1) as b:
                batch(b)
            batch(B - 1)
            end = UNITS * B
            normalise(end - 2, True)
            reciprocals(end - 1, 1, True)
            normalise(end - 1, True)

        @block.sync
        def _(sp):
            def stack(pairno, par, j, fbuf, number_):
                which, h = KINDS[j]
                sp.wait_ge(s_split, number_ + 1)
                cols = slice(h * HALF, (h + 1) * HALF)
                for head in range(2):
                    rows = slice(head * HD, (head + 1) * HD)
                    high, low = hs[rows, j % 2, :], fl[rows, fbuf, :]
                    if which == "k":
                        moves = [(k_hi[r, par, head, cols], high) for r in (slice(0, HD), slice(HD, P))]
                        moves += [(k_lo[r, par, head, cols], low) for r in (slice(0, HD), slice(HD, P))]
                    elif h == 0:
                        moves = [(q0[0:HD, head, :], high), (q0[HD:P, head, :], low)]
                    else:
                        moves = [(q1[0:HD, par, head, :], high), (q1[HD:P, par, head, :], low)]
                    for dst, src in moves:
                        sp.dma_start(dst.bitcast(F32), src).then_inc(s_stk[j % 2], 16)

            def load_x(b):
                hold(sp)
                sp.dma_start(xs[:], xv[b]).then_inc(s_x_in, 16)

            def chunk_view(dram, b, r8):
                ot, h = r8 % 4, r8 // 4
                return dram[b, :, ot, h * HALF:(h + 1) * HALF]

            def buf(r8):
                return hs[:, r8 % 2, :]

            def load_residual(b, r8):
                hold(sp)
                sp.dma_start(buf(r8), chunk_view(xv, b, r8)).then_inc(s_res[r8 % 2], 16)

            def store(b, r8):
                hold(sp)
                sp.dma_start(chunk_view(ov, b, r8), buf(r8)).then_inc(s_out[r8 % 2], 16)

            sp.dma_start(fl[:, 0, :], gamma.rearrange("(o c) -> o c", o=1).broadcast_to([P, C])).then_inc(s_par_in, 16)
            sp.dma_start(fl[:, 1, :], beta.rearrange("(o c) -> o c", o=1).broadcast_to([P, C])).then_inc(s_par_in, 16)
            sp.dma_start(bias[:, 0:12], qkv_b.rearrange("(t p) -> p t", p=P), allow_slow_non_contiguous=True).then_inc(s_par_in, 16)
            sp.dma_start(bias[:, 12:16], proj_b.rearrange("(t p) -> p t", p=P), allow_slow_non_contiguous=True).then_inc(s_par_in, 16)
            for t in range(WT_TILES):
                if t == 2:
                    load_x(0)
                if t >= 2:
                    sp.wait_ge(s_setup, setup_at["wn_free", t - 2])
                src = qkv_w[t * P:(t + 1) * P, :] if t < 12 else proj_w[(t - 12) * P:(t - 11) * P, :]
                sp.dma_start(hs[:, t % 2, :], src).then_inc(s_w_in[t % 2], 16)
            for j in range(4):
                stack(0, 0, j, j % 2, j)

            def batch(b):
                first, last = isinstance(b, int) and b == 0, isinstance(b, int) and b == B - 1
                if not last:
                    sp.wait_ge(s_xlo, CB * (b + 1))
                    load_x(b + 1)
                for m in range(NCH):
                    kind, db, what = slot(b, m)
                    if not active(b, m):
                        continue
                    c = number(b, m)
                    if kind == QK:
                        pairno = (b + db) * PAIRS + what[0]
                        j = what[1]
                        if not (first and what[0] == 1 and db == 0 and j != 3):
                            sp.wait_ge(s_scores, 16 * (pairno - 1) + (8 if j == 3 else 0))
                            hold(sp)
                        stack(pairno, what[0] % 2, j, m % 2, c)
                        if j == 3 and 0 < m // 8 < 3 and not first:
                            for r in range(2):
                                sp.wait_ge(s_stk[r], stacked(pairno, 2 + r))
                                load_residual(b - 1, (m // 8 - 1) * 4 + r)
                    if kind == PROJ:
                        sp.wait_ge(s_split, c + 1)
                        store(b - 1, what)
                        if what % 4 < 2:
                            sp.wait_ge(s_out[what % 2], 16 * (4 * (b - 1) + what // 2 + 1))
                            load_residual(b - 1, what + 2)

            batch(0)
            with sp.Fori(1, B - 1) as b:
                batch(b)
            batch(B - 1)
            for r in range(8):
                if r == 0:
                    load_residual(B - 1, 0)
                    load_residual(B - 1, 1)
                sp.wait_ge(s_split, NCH * (B - 1) + 24 + r + 1)
                store(B - 1, r)
                if r < 6:
                    sp.wait_ge(s_out[r % 2], 16 * (4 * (B - 1) + r // 2 + 1))
                    load_residual(B - 1, r + 2)
            for r in range(2):
                sp.wait_ge(s_out[r], 16 * 4 * B)

        @block.gpsimd
        def _(pool):
            pool.memset(ident[:], 0.0).then_inc(s_const, 1)
            pool.memset(grp[:], GROUPS / C).then_inc(s_const, 1)
            pool.memset(inv[:, 8:12], V_SCALE).then_inc(s_const, 1)
            pool.wait_ge(s_const, 3)
            pool.affine_select(out=ident[:], in_=ident[:], compare_op=ALU.not_equal, fill=1.0, base=0,
                               pattern=[[-1, P]], channel_multiplier=1).then_inc(s_const, 1)
            g3 = grp[:].rearrange("p (g j) -> p g j", j=C // GROUPS)
            pool.affine_select(out=g3, in_=g3, compare_op=ALU.is_ge, fill=0.0, base=0,
                               pattern=[[-(C // GROUPS), P * GROUPS // C], [0, C // GROUPS]],
                               channel_multiplier=1).then_inc(s_const, 1)
            pool.wait_ge(s_const, 5)
            pool.affine_select(out=g3, in_=g3, compare_op=ALU.is_ge, fill=0.0, base=C // GROUPS - 1,
                               pattern=[[C // GROUPS, P * GROUPS // C], [0, C // GROUPS]],
                               channel_multiplier=-1).then_inc(s_const, 1)

            def x_low(b, c):
                pool.wait_ge(s_stat, STAT * b + X_HIGH + 2 * c)
                pool.tensor_tensor(xn_lo[:, c, :], xs[:, c, :], xn_hi[:, c, :], ALU.subtract).then_inc(s_xlo, 1)

            def split(b, kind, what, c, f, n, vno, proj_r):
                pool.wait_ge(s_ev, c + 1)
                hold(pool)
                if kind == QK:
                    j = what[1]
                    pool.tensor_copy(hs[:, j % 2, :].bitcast(F32R), fl[:, f, :]).then_inc(s_qkh, 1)
                    pool.wait_ge(s_qkh, n + 1)
                    pool.tensor_tensor(fl[:, f, :].bitcast(F32R), fl[:, f, :], hs[:, j % 2, :],
                                       ALU.subtract).then_inc(s_split, 1)
                elif kind == V:
                    g, j = what
                    dst = [v[:, 2 * j:2 * j + 2, g * 256:(g + 1) * 256] for v in (v_hi, v_lo)]
                    src = fl[:, f, :].rearrange("p (s d) -> p s d", s=2)
                    pool.tensor_copy(dst[0], src).then_inc(s_vh, 1)
                    pool.wait_ge(s_vh, vno + 1)
                    pool.tensor_tensor(dst[1], src, dst[0], ALU.subtract).then_inc(s_split, 1)
                else:
                    r = what
                    pool.wait_ge(s_res[r % 2], 16 * (proj_r * 4 + r // 2 + 1))
                    pool.tensor_tensor(hs[:, r % 2, :], fl[:, f, :], hs[:, r % 2, :], ALU.add).then_inc(s_split, 1)

            def out_split(unit, par, u):
                p, q = divmod(u, 4)
                pool.wait_ge(s_norm, unit + 1)
                hold(pool)
                at = bass.ds(par * (CB * T) + (p * T + q * QT), QT)
                pool.tensor_copy(on_hi[:, at], onorm[:]).then_inc(s_onh, 1)
                pool.wait_ge(s_onh, unit + 1)
                pool.tensor_tensor(on_lo[:, at], onorm[:], on_hi[:, at], ALU.subtract).then_inc(s_on, 1)

            for c in range(CB):
                x_low(0, c)
            for c, (kind, what) in enumerate(PRE_CHUNKS):
                if kind == QK and c >= 2:
                    pool.wait_ge(s_stk[c % 2], stacked(0, c - 2))
                split(0, kind, what, c, c % 2, c, c - 4, 0)

            def batch(b):
                first, last = isinstance(b, int) and b == 0, isinstance(b, int) and b == B - 1
                for k in range(STEPS):
                    if k % 2 == 0:
                        m = k // 2 - 1 if k else NCH - 1
                        if k and active(b, m):
                            kind, db, what = slot(b, m)
                            if kind == QK:
                                pairno, j = (b + db) * PAIRS + what[0], what[1]
                                if j >= 2:
                                    pool.wait_ge(s_stk[j % 2], stacked(pairno, j - 2))
                                elif m // 8 < 2 or first:
                                    pool.wait_ge(s_stk[j % 2], stacked(pairno - 1, 2 + j))
                                else:
                                    pool.wait_ge(s_out[j % 2], 16 * (4 * (b - 1) + 2 * (m // 8 - 1)))
                                split(b, kind, what, number(b, m), m % 2, qk_number(b, m), 0, 0)
                            elif kind == V:
                                if what[1] == 0 and not (first and db == 0):
                                    pool.wait_ge(s_pv, UNITS * b + (8 if db else 0))
                                split(b, kind, what, number(b, m), m % 2, 0, v_number(b, m), 0)
                            else:
                                split(b, kind, what, number(b, m), m % 2, 0, 0, b - 1)
                        if k == 0 and not first:
                            split(b, V, (0, 3), NCH * b - 1, 1, 0, b * 8 + 3, 0)
                    if k % 4 == 0:
                        u = k // 4
                        if u >= 2:
                            out_split(UNITS * b + u - 2, parity(b), u - 2)
                        elif not first:
                            out_split(UNITS * b + u - 2, parity(b + 1), UNITS + u - 2)
                    if not last and 43 <= k < 43 + CB:
                        x_low(b + 1, k - 43)

            batch(0)
            with pool.Fori(1, B - 1) as b:
                batch(b)
            batch(B - 1)
            for u in (UNITS - 2, UNITS - 1):
                out_split(UNITS * (B - 1) + u, parity(B - 1), u)
            for r in range(8):
                split(B - 1, PROJ, r, NCH * (B - 1) + 24 + r, r % 2, 0, 0, B - 1)

        @block.scalar
        def _(act):
            for t in range(WT_TILES):
                act.wait_ge(s_wtr, t + 1)
                act.activation(wt_hi[:, :, t * P:(t + 1) * P], weight_bank(t), ACT.Copy).then_inc(s_wh, 1)

            def evacuate(c, f, kind, what):
                act.wait_ge(s_chunk, c + 1)
                t = tiles_of(kind, what)
                act.activation(fl[:, f, :], mix[:], ACT.Identity, scale=inv[:, t:t + 1],
                               bias=bias[:, t:t + 1]).then_inc(s_ev, 1)

            def exp(K, buf, again, ubuf, i, unit):
                act.wait_ge(s_max, K + 1)
                if again:
                    act.wait_ge(s_rcp, unit - 1)
                act.activation(prob[:, buf, :], scores[:, buf, :], ACT.Exp, bias=nmax[:, buf:buf + 1], scale=1.0,
                               accum_out=sums[:, ubuf, i:i + 1]).then_inc(s_exp, 1)

            def high(K, head, tt, half, ubuf):
                act.wait_ge(s_tr, 2 * K + half + 1)
                dst = pt_hi[:, ubuf, head, 4 * half:4 * half + 4, tt * P:(tt + 1) * P]
                act.activation(dst, tr[:, half], ACT.Copy, scale=P_SCALE).then_inc(s_phi, 1)

            act.wait_ge(s_setup, setup_at["done"])
            act.wait_ge(s_const, 6)
            for c, (kind, what) in enumerate(PRE_CHUNKS):
                if 2 <= c < 6:
                    act.wait_ge(s_stk[c % 2], stacked(0, c - 2))
                if c >= 6:
                    act.wait_ge(s_split, c - 1)
                evacuate(c, c % 2, kind, what)
            exp(0, 0, False, 0, 0, 0)
            exp(1, 1, False, 0, 1, 0)

            def batch(b):
                first, last = isinstance(b, int) and b == 0, isinstance(b, int) and b == B - 1
                for k in range(STEPS):
                    K, u, i = STEPS * b + k, k // 4, k % 4
                    if k == 0 and not first:
                        act.wait_ge(s_split, NCH * b - 2)
                        evacuate(NCH * b - 1, 1, V, (0, 3))
                    if k and k % 2 == 0 and active(b, k // 2 - 1):
                        m = k // 2 - 1
                        kind, db, what = slot(b, m)
                        c = number(b, m)
                        before = m - 2
                        while before >= 0 and not active(b, before):
                            before -= 2
                        if before >= 0 and slot(b, before)[0] == QK:
                            _, pdb, (pp, pj) = slot(b, before)
                            act.wait_ge(s_stk[pj % 2], stacked((b + pdb) * PAIRS + pp, pj))
                        else:
                            act.wait_ge(s_split, c - 1)
                        evacuate(c, m % 2, kind, what)
                    if i == 0 and not (first and u < 2):
                        act.wait_ge(s_pv, UNITS * b + u - 1)
                    for half in range(2):
                        high(K, i // 2, i % 2, half, u % 2)
                    if not (last and k >= STEPS - 2):
                        u2, i2 = divmod(k + 2, 4)
                        exp(K + 2, k % 2, i2 == 0 and not (first and u2 < 2), u2 % 2, i2, UNITS * b + u2)

            batch(0)
            with act.Fori(1, B - 1) as b:
                batch(b)
            batch(B - 1)
            for r in range(8):
                c = NCH * (B - 1) + 24 + r
                act.wait_ge(s_split, c - 1)
                evacuate(c, r % 2, PROJ, r)

        @block.tensor
        def _(pe):
            pe.wait_ge(s_const, 6)
            for t in range(WT_TILES):
                if t == 12:
                    pe.wait_ge(s_setup, setup_at["spread"])
                    for i in range(4):
                        pe.transpose(mix[:, i * P:(i + 1) * P], prob[:, 0, i * P:(i + 1) * P], ident[:])
                    for i in range(4):
                        last_t = pe.transpose(acc[:].rearrange("p a b -> p (a b)")[:, i * P:(i + 1) * P],
                                              prob[:, 0, (4 + i) * P:(5 + i) * P], ident[:])
                    last_t.then_inc(s_rowb, 1)
                pe.wait_ge(s_setup, setup_at["wm", t])
                if t >= 4:
                    pe.wait_ge(s_wl, t - 3)
                for c in range(CB):
                    col = (t % 2) * C + c * P
                    tp = pe.transpose(weight_bank(t)[:, c], prob[:, 1, col:col + P], ident[:])
                tp.then_inc(s_wtr, 1)

            TERMS = [("h", "h"), ("h", "l"), ("l", "h")]
            WTT = {"h": wt_hi, "l": wt_lo}
            XN = {"h": xn_hi, "l": xn_lo}
            ON = {"h": on_hi, "l": on_lo}

            def chunk_half(kind, what, half, par=0):
                if kind == V:
                    g, j = what
                    s = 2 * j + half
                    for n, (a, w) in enumerate(TERMS):
                        for c in range(CB):
                            mm = pe.matmul(mix[:, half * 256:(half + 1) * 256], XN[a][:, c, s * P:(s + 1) * P],
                                           WTT[w][:, c, 2 * C + g * 256:2 * C + (g + 1) * 256],
                                           start=(n == 0 and c == 0), stop=(n == 2 and c == CB - 1))
                    return mm
                t = tiles_of(kind, what)
                h = KINDS[what[1]][1] if kind == QK else what // 4
                for e in range(6 * half, 6 * half + 6):
                    (w, a), c = TERMS[e // CB], e % CB
                    if kind == QK:
                        rhs = XN[a][:, c, h * HALF:(h + 1) * HALF]
                    else:
                        rhs = ON[a][:, bass.ds(par * (CB * T) + (c * T + h * HALF), HALF)]
                    mm = pe.matmul(mix[:], WTT[w][:, c, t * P:(t + 1) * P], rhs, start=(e == 0), stop=(e == 11))
                return mm

            def group_sums(b):
                pe.wait_ge(s_stat, STAT * b + GROUP_IN)
                pe.matmul(mix[:, 0:8], grp[:], xstat[:, 56:64], start=True, stop=True).then_inc(s_gsum, 1)
                pe.wait_ge(s_stat, STAT * b + GROUP_OUT)

            def step_scores(k, buf):
                p, s = divmod(k % STEPS, 16)
                tile_, head = 2 * (s // 4) + s % 2, (s % 4) // 2
                lhs = q0[:, head, tile_ * P:(tile_ + 1) * P] if tile_ < 4 else \
                    q1[:, p % 2, head, (tile_ - 4) * P:(tile_ - 3) * P]
                for sh in range(2):
                    cols = slice(sh * HALF, (sh + 1) * HALF)
                    for n, kk in enumerate((k_hi, k_lo)):
                        mm = pe.matmul(scores[:, buf, cols], lhs, kk[:, p % 2, head, cols],
                                       start=(n == 0), stop=(n == 1))
                mm.then_inc(s_scores, 1)

            def pair_ready(pairno):
                for r in range(2):
                    pe.wait_ge(s_stk[r], 192 * (pairno + 1))

            def step_transposes(K, buf, waits):
                for half in range(2):
                    if waits:
                        pe.wait_ge(s_plo, 2 * K - 1 + half)
                    for j in range(4):
                        s = 4 * half + j
                        tp = pe.transpose(tr[:, half, j, :], prob[:, buf, s * P:(s + 1) * P], ident[:])
                    tp.then_inc(s_tr, 1)

            def prob_v(ubuf, u, i):
                for s in (2 * i, 2 * i + 1):
                    for n, (pt, v) in enumerate(((pt_hi, v_hi), (pt_lo, v_hi), (pt_hi, v_lo))):
                        for head in range(2):
                            d = (2 * (u // 4) + head) * HD
                            mm = pe.matmul(acc[head * HD:(head + 1) * HD, 0, :], v[:, s, d:d + HD],
                                           pt[:, ubuf, head, s, :], start=(s == 0 and n == 0),
                                           stop=(s == ST - 1 and n == 2))
                return mm

            def unit_sums(unit):
                pe.wait_ge(s_rb, unit + 1)
                for tt in range(2):
                    tp = pe.transpose(acc[:, 1, tt * P:(tt + 1) * P], rb[:, tt].rearrange("p a b -> p (a b)"), ident[:])
                tp.then_inc(s_rt, 1)

            pe.wait_ge(s_setup, setup_at["done"])
            group_sums(0)
            pe.wait_ge(s_xlo, CB)
            pe.wait_ge(s_wl, WT_TILES)
            for c, (kind, what) in enumerate(PRE_CHUNKS):
                if c:
                    pe.wait_ge(s_ev, c)
                chunk_half(kind, what, 0)
                chunk_half(kind, what, 1).then_inc(s_chunk, 1)
            pair_ready(0)
            step_scores(0, 0)
            step_scores(1, 1)

            def batch(b):
                first, last = isinstance(b, int) and b == 0, isinstance(b, int) and b == B - 1
                for k in range(STEPS):
                    K, u, i, m = STEPS * b + k, k // 4, k % 4, k // 2
                    pe.wait_ge(s_exp, K + 1)
                    if not (last and k >= STEPS - 2):
                        if (k + 2) % 16 == 0:
                            pair_ready(PAIRS * b + (k + 2) // 16)
                        step_scores(k + 2, k % 2)
                    step_transposes(K, k % 2, not (first and k == 0))

                    def chunk():
                        if not active(b, m):
                            return
                        kind, db, what = slot(b, m)
                        c = number(b, m)
                        if k % 2 == 0:
                            pe.wait_ge(s_ev, c)
                            if kind == QK and m == 24:
                                pe.wait_ge(s_xlo, CB * (b + 2))
                            if kind == PROJ:
                                pe.wait_ge(s_on, UNITS * b)
                        mm = chunk_half(kind, what, k % 2, parity(b + 1))
                        if k % 2:
                            mm.then_inc(s_chunk, 1)

                    if k != 40:
                        chunk()
                    if not (first and u == 0):
                        if i == 0:
                            if not (first and u == 1):
                                pe.wait_ge(s_norm, UNITS * b + u - 1)
                            pe.wait_ge(s_plo, 2 * K)
                            if u == 1:
                                pe.wait_ge(s_split, PRE if first else NCH * b)
                            if u == 9:
                                pe.wait_ge(s_split, number(b, 7) + 1)
                        mm = prob_v((u - 1) % 2, (u - 1) % UNITS, i)
                        if i == 3:
                            mm.then_inc(s_pv, 1)
                            unit_sums(UNITS * b + u - 1)
                    if k == 40:
                        if not last:
                            pe.wait_ge(s_ev, number(b, 19) + 1)
                            group_sums(b + 1)
                        chunk()

            batch(0)
            with pe.Fori(1, B - 1) as b:
                batch(b)
            batch(B - 1)
            end = UNITS * B
            pe.wait_ge(s_norm, end - 1)
            pe.wait_ge(s_plo, 8 * end)
            for i in range(4):
                mm = prob_v(1, UNITS - 1, i)
            mm.then_inc(s_pv, 1)
            unit_sums(end - 1)
            pe.wait_ge(s_on, end)
            for r in range(8):
                pe.wait_ge(s_ev, NCH * (B - 1) + 24 + r)
                chunk_half(PROJ, r, 0, parity(B - 1))
                chunk_half(PROJ, r, 1, parity(B - 1)).then_inc(s_chunk, 1)


def kernel(**inputs):
    import numpy as np
    import concourse.bacc as bacc
    from concourse import mybir as mb
    from concourse.bass_utils import run_bass_kernel_spmd as run

    names = ["x", "L0_conv_gn_gamma", "L0_conv_gn_beta", "L0_conv_qkv_w", "L0_conv_qkv_b", "L0_conv_proj_w",
             "L0_conv_proj_b"]
    nc = bacc.Bacc("TRN2", target_bir_lowering=False, num_devices=1)
    arrays, args = {}, []
    for name in names:
        a = np.ascontiguousarray(inputs[name])
        arrays[f"in_{name}"] = a
        args.append(nc.dram_tensor(f"in_{name}", a.shape, mb.dt.from_np(a.dtype), kind="ExternalInput").ap())
    shape = np.shape(inputs["x"])
    args.append(nc.dram_tensor("out_0", shape, mb.dt.float32, kind="ExternalOutput").ap())
    attention_block(nc, *args)
    r = run(nc, [arrays], core_ids=[0])
    return r.results[0]["out_0"]
```

```python
from contextlib import ExitStack

import concourse.bass as bass
from concourse import mybir

F32 = mybir.dt.float32
F32R = mybir.dt.float32r
F16 = mybir.dt.float16
U32 = mybir.dt.uint32
I32 = mybir.dt.int32
ALU = mybir.AluOpType
ACT = mybir.ActivationFunctionType
AX = mybir.AxisListType

P = 128
HEADS = 8
GROUPS = 32
EPS = 1e-5
X_SCALE = 2.0 ** 8
W_TOP = 2.0 ** 14
V_SCALE = 2.0 ** -15
P_SCALE = 2.0 ** 15


def attention_block(nc, x, gamma, beta, qkv_w, qkv_b, proj_w, proj_b, out):
    B, C, HGT, WID = x.shape
    T = HGT * WID
    CB = C // P
    HD = C // HEADS
    PAIRS = HEADS // 2
    HALF = T // 2
    QT = T // 4
    ST = T // P
    WT_TILES = 4 * CB
    STEPS = HEADS * ST
    UNITS = STEPS // 4
    PRE = 8
    NCH = 32
    STAT = 43
    GROUP_IN, GROUP_OUT, X_HIGH = 15, 16, 37
    SCALE_Q = float(HD) ** -0.5
    assert T == 1024 and C == 512 and HD == 64 and SCALE_Q == 0.125

    xv = x.rearrange("b (c p) h w -> b p c (h w)", p=P)
    ov = out.rearrange("b (c p) h w -> b p c (h w)", p=P)

    with ExitStack() as ctx:
        def sb(name, shape, dt):
            return ctx.enter_context(nc.sbuf_tensor(name, shape, dt))

        def sem(name):
            return ctx.enter_context(nc.semaphore(name))

        wt_hi = sb("wt_hi", [P, CB, WT_TILES * P], F16)
        wt_lo = sb("wt_lo", [P, CB, WT_TILES * P], F16)
        pt_hi = sb("pt_hi", [P, 2, 2, ST, QT], F16)
        pt_lo = sb("pt_lo", [P, 2, 2, ST, QT], F16)
        xn_hi = sb("xn_hi", [P, CB, T], F16)
        xn_lo = sb("xn_lo", [P, CB, T], F16)
        xs = sb("xs", [P, CB, T], F32)
        q0 = sb("q0", [P, 2, HALF], F32R)
        q1 = sb("q1", [P, 2, 2, HALF], F32R)
        k_hi = sb("k_hi", [P, 2, 2, T], F32R)
        k_lo = sb("k_lo", [P, 2, 2, T], F32R)
        v_hi = sb("v_hi", [P, ST, C], F16)
        v_lo = sb("v_lo", [P, ST, C], F16)
        prob = sb("prob", [P, 2, T], F32)
        on_hi = sb("on_hi", [P, 2 * CB * T], F16)
        on_lo = sb("on_lo", [P, 2 * CB * T], F16)
        fl = sb("fl", [P, 2, HALF], F32)
        hs = sb("hs", [P, 2, HALF], F32)
        onorm = sb("onorm", [P, QT], F32)
        rb = sb("rb", [P, 2, 2, HD], F32)
        ident = sb("ident", [P, P], F32)
        grp = sb("grp", [P, P], F32)
        inv = sb("inv", [P, WT_TILES + 1], F32)
        bias = sb("bias", [P, WT_TILES + 1], F32)
        small = sb("small", [P, 64], F32)
        xstat = sb("xstat", [P, 96], F32)
        sums = sb("sums", [P, 2, 4], F32)
        tot, pw, rc = [small[:, i * WT_TILES:(i + 1) * WT_TILES] for i in range(3)]
        rcp = small[:, 56:60]
        nmax = small[:, 60:62]

        scores = ctx.enter_context(nc.psum_tensor("scores", [P, 2, T], F32))
        tr = ctx.enter_context(nc.psum_tensor("tr", [P, 2, 4, P], F32))
        acc = ctx.enter_context(nc.psum_tensor("acc", [P, 2, QT], F32))
        mix = ctx.enter_context(nc.psum_tensor("mix", [P, HALF], F32))

        s_w_in = [sem("s_w_in0"), sem("s_w_in1"), sem("s_w_in2")]
        s_par_in = sem("s_par_in")
        s_const = sem("s_const")
        s_setup = sem("s_setup")
        s_wsum = sem("s_wsum")
        s_wsc = sem("s_wsc")
        s_wtr = sem("s_wtr")
        s_wh = sem("s_wh")
        s_wl = sem("s_wl")
        s_rowb = sem("s_rowb")
        s_x_in = sem("s_x_in")
        s_stat = sem("s_stat")
        s_gsum = sem("s_gsum")
        s_xlo = sem("s_xlo")
        s_scores = sem("s_scores")
        s_max = sem("s_max")
        s_exp = sem("s_exp")
        s_tr = sem("s_tr")
        s_phi = sem("s_phi")
        s_plo = sem("s_plo")
        s_pv = sem("s_pv")
        s_rcp = sem("s_rcp")
        s_rb = sem("s_rb")
        s_rt = sem("s_rt")
        s_rs = sem("s_rs")
        s_norm = sem("s_norm")
        s_onh = sem("s_onh")
        s_on = sem("s_on")
        s_held = sem("s_held")
        s_chunk = sem("s_chunk")
        s_ev = sem("s_ev")
        s_qkh = sem("s_qkh")
        s_vh = sem("s_vh")
        s_split = sem("s_split")
        s_stk = [sem("s_stk0"), sem("s_stk1")]
        s_res = [sem("s_res0"), sem("s_res1")]
        s_out = [sem("s_out0"), sem("s_out1")]

        QK, V, PROJ = "qk", "v", "proj"
        KINDS = [("k", 0), ("k", 1), ("q", 1), ("q", 0)]

        def slot(b, m):
            w, j = divmod(m, 8)
            if j < 4:
                return (QK, int(w == 3), ((w + 1) % PAIRS, j))
            if w in (0, 3):
                return (V, int(w == 3), (int(w == 0), j - 4))
            return (PROJ, -1, (w - 1) * 4 + j - 4)

        def active(b, m):
            kind, db, _ = slot(b, m)
            if isinstance(b, int):
                return 0 <= b + db < B
            return True

        def number(b, m):
            if isinstance(b, int) and b == 0:
                return PRE + sum(active(0, j) for j in range(m))
            return NCH * b + m

        def qk_number(b, m):
            _, db, (p, j) = slot(b, m)
            return (b + db) * 4 * PAIRS + 4 * p + j

        def v_number(b, m):
            _, db, (g, j) = slot(b, m)
            return (b + db) * 8 + 4 * g + j

        def stacked(pair, j):
            return pair * 192 + (128 if j < 2 else 192)

        def parity(b):
            return b % 2

        def tiles_of(kind, what):
            if kind == QK:
                p, j = what
                return (4 + p) if KINDS[j][0] == "k" else p
            return WT_TILES if kind == V else 12 + what % 4

        ORDER = [4, 0, 8, 9, 5, 1, 10, 11, 6, 2, 7, 3, 12, 13, 14, 15]
        assert sorted(ORDER) == list(range(WT_TILES))
        TILES_AFTER = [1, 2, 1, 2, 1, 2, 1, 3]
        FIRST_AFTER = [3 + sum(TILES_AFTER[:c]) for c in range(PRE)]
        assert 3 + sum(TILES_AFTER) == WT_TILES
        WRING = 3

        def scratch(tensor, i):
            flat = tensor[:].rearrange("p u h s t -> p (u h s t)")
            return flat[:, 2 * i * HALF:2 * (i + 1) * HALF].bitcast(F32)

        raw_weights = [scratch(pt_hi, i) for i in range(WRING)]
        scaled_weights = [scratch(pt_hi, WRING + i) for i in range(WRING)]
        junk_dve, junk_act = scratch(pt_hi, 6), scratch(pt_hi, 7)
        gamma_row, beta_row = scratch(pt_lo, 0), scratch(pt_lo, 1)
        pre_fl = [scratch(pt_lo, 2 + i) for i in range(4)] + [fl[:, 0, :], fl[:, 1, :],
                                                              prob[:, 1, 0:HALF], prob[:, 1, HALF:T]]
        pre_hs = [scratch(pt_lo, 6), scratch(pt_lo, 7), hs[:, 0, :], hs[:, 1, :]]
        pre_bank = [mix[:], acc[:].rearrange("p a b -> p (a b)")]
        v_scale_row, v_bias_row = [tr[:, i].rearrange("p a b -> p (a b)") for i in range(2)]

        def weight_bank(n):
            bank = scores[:, (n // 2) % 2, (n % 2) * HALF:(n % 2 + 1) * HALF]
            return bank.rearrange("p (c o) -> p c o", c=CB)

        def hold(engine):
            engine.sem_inc(s_held, 1)

        PRE_CHUNKS = [(QK, (0, j)) for j in range(4)] + [(V, (0, j)) for j in range(4)]

        block = ctx.enter_context(nc.Block())

        setup_at = {}

        @block.vector
        def _(dve):
            count = [0]

            def mark(ins):
                ins.then_inc(s_setup, 1)
                count[0] += 1
                return count[0]

            spread_cols, guarded, dots = small[:, 48:52], small[:, 52:54], small[:, 54:56]

            def product(n):
                dve.wait_ge(s_w_in[n % WRING], 16 * (n // WRING + 1))
                if n >= WRING:
                    dve.wait_ge(s_wtr, n - WRING + 1)
                setup_at["product", n] = mark(dve.tensor_tensor(
                    scaled_weights[n % WRING], raw_weights[n % WRING],
                    gamma_row if ORDER[n] < 12 else v_scale_row, ALU.mult))

            def dot(n):
                if n >= 2:
                    dve.wait_ge(s_setup, setup_at["biased", n - 2])
                elif n:
                    dve.wait_ge(s_setup, setup_at["dot", n - 1])
                setup_at["dot", n] = mark(dve.tensor_tensor_reduce(
                    out=junk_dve, in0=raw_weights[n % WRING], in1=beta_row if ORDER[n] < 12 else v_bias_row,
                    scale=1.0, scalar=0.0, op0=ALU.mult, op1=ALU.add, accum_out=dots[:, n % 2:n % 2 + 1]))

            def guard(n):
                dve.wait_ge(s_wsum, n + 1)
                t = ORDER[n]
                setup_at["guard", n] = mark(dve.tensor_scalar(guarded[:, n % 2:n % 2 + 1], tot[:, t:t + 1],
                                                              2.0 ** -100, None, ALU.max))

            def power(n):
                t = ORDER[n]
                dve.wait_ge(s_setup, setup_at["guard", n])
                setup_at["power", n] = mark(dve.tensor_scalar(
                    pw[:, t:t + 1].bitcast(U32), guarded[:, n % 2:n % 2 + 1].bitcast(U32), 0x7F800000, None,
                    ALU.bitwise_and))

            def inverse(n):
                t = ORDER[n]
                dve.wait_ge(s_setup, setup_at["power", n])
                setup_at["inverse", n] = mark(dve.reciprocal(rc[:, t:t + 1], pw[:, t:t + 1]))

            def undo(n):
                t = ORDER[n]
                if t // 4 != 2:
                    factor = (SCALE_Q / (W_TOP * X_SCALE), 1.0 / (W_TOP * X_SCALE), None, 1.0 / W_TOP)[t // 4]
                    mark(dve.tensor_scalar(inv[:, t:t + 1], pw[:, t:t + 1], factor, None, ALU.mult))
                dve.wait_ge(s_setup, setup_at["dot", n])
                setup_at["biased", n] = mark(dve.tensor_tensor(bias[:, t:t + 1], bias[:, t:t + 1],
                                                               dots[:, n % 2:n % 2 + 1], ALU.add))
                if t < 4:
                    dve.wait_ge(s_setup, setup_at["biased", n])
                    mark(dve.tensor_scalar(bias[:, t:t + 1], bias[:, t:t + 1], SCALE_Q, None, ALU.mult))
                setup_at["undo", n] = count[0]

            def low_weights(n):
                dve.wait_ge(s_wh, n + 1)
                cols = slice(ORDER[n] * P, (ORDER[n] + 1) * P)
                dve.scalar_tensor_tensor(out=wt_lo[:, :, cols], in0=weight_bank(n), scalar=W_TOP,
                                         in1=wt_hi[:, :, cols], op0=ALU.mult, op1=ALU.subtract).then_inc(s_wl, 1)

            def spread_v():
                dve.wait_ge(s_setup, setup_at["undo", 7])
                at = mark(dve.tensor_scalar(spread_cols, pw[:, 8:12], 1.0 / (W_TOP * X_SCALE * V_SCALE),
                                            None, ALU.mult))
                dve.wait_ge(s_setup, at)
                for i in range(4):
                    mark(dve.tensor_scalar(prob[:, 0, i * P:(i + 1) * P], ident[:], 0.0,
                                           spread_cols[:, i:i + 1], ALU.mult, ALU.add))
                    mark(dve.tensor_scalar(prob[:, 0, (4 + i) * P:(5 + i) * P], ident[:], 0.0,
                                           bias[:, 8 + i:9 + i], ALU.mult, ALU.add))
                setup_at["spread"] = count[0]

            bns = xstat[:, 0:48].rearrange("p (n s) -> p n s", s=6)
            mv = xstat[:, 48:56].rearrange("p (c s) -> p c s", s=2)
            gin, gout = xstat[:, 56:64], xstat[:, 64:72]
            t1, var, t3, y, a_x, b_x = [xstat[:, 72 + 4 * i:76 + 4 * i] for i in range(6)]

            class Norm:
                def __init__(self, b):
                    self.b, self.base, self.n = b, STAT * b, 0

                def mark(self, ins):
                    ins.then_inc(s_stat, 1)
                    self.n += 1

                def settle(self):
                    dve.wait_ge(s_stat, self.base + self.n)

                def stats(self, part):
                    if part == 0:
                        dve.wait_ge(s_x_in, 16 * (self.b + 1))
                    c, h = divmod(part, 2)
                    self.mark(dve.bn_stats(bns[:, part, :], xs[:, c, h * HALF:(h + 1) * HALF]))

                def channel_means(self):
                    self.settle()
                    hold(dve)
                    for c in range(CB):
                        self.mark(dve.bn_aggr(mv[:, c, :], bns[:, 2 * c:2 * c + 2, :]))
                    self.settle()
                    self.mark(dve.tensor_tensor(t1, mv[:, :, 0], mv[:, :, 0], ALU.mult))
                    self.settle()
                    self.mark(dve.tensor_tensor(gin[:, 4:8], t1, mv[:, :, 1], ALU.add))
                    self.mark(dve.tensor_copy(gin[:, 0:4], mv[:, :, 0]))
                    assert self.n == GROUP_IN

                def group_out(self):
                    dve.wait_ge(s_gsum, self.b + 1)
                    self.mark(dve.tensor_copy(gout, acc[:, 1, 0:8]))
                    assert self.n == GROUP_OUT

                def variance(self):
                    mean = gout[:, 0:4]
                    self.settle()
                    self.mark(dve.tensor_tensor(t1, mean, mean, ALU.mult))
                    self.settle()
                    self.mark(dve.tensor_tensor(var, gout[:, 4:8], t1, ALU.subtract))
                    self.settle()
                    self.mark(dve.tensor_scalar(var, var, 0.0, EPS, ALU.max, ALU.add))
                    self.settle()
                    self.mark(dve.tensor_scalar(t1.bitcast(U32), var.bitcast(U32), 1, None, ALU.logical_shift_right))
                    self.settle()
                    self.mark(dve.tensor_scalar(y.bitcast(I32), t1.bitcast(I32), -1.0, float(0x5F3759DF),
                                                ALU.mult, ALU.add))

                def newton(self):
                    self.settle()
                    self.mark(dve.tensor_tensor(t1, y, y, ALU.mult))
                    self.settle()
                    self.mark(dve.tensor_tensor(t3, t1, var, ALU.mult))
                    self.settle()
                    self.mark(dve.tensor_scalar(t1, t3, -0.5, 1.5, ALU.mult, ALU.add))
                    self.settle()
                    self.mark(dve.tensor_tensor(y, y, t1, ALU.mult))

                def factors(self):
                    self.settle()
                    self.mark(dve.tensor_scalar(a_x, y, X_SCALE, None, ALU.mult))
                    self.settle()
                    self.mark(dve.scalar_tensor_tensor(out=b_x, in0=gout[:, 0:4], scalar=-1.0, in1=a_x,
                                                       op0=ALU.mult, op1=ALU.mult))

                def apply(self, c):
                    self.settle()
                    self.mark(dve.tensor_scalar(xs[:, c, :], xs[:, c, :], a_x[:, c:c + 1], b_x[:, c:c + 1],
                                                ALU.mult, ALU.add))
                    self.settle()
                    self.mark(dve.tensor_copy(xn_hi[:, c, :], xs[:, c, :]))
                    assert self.n == X_HIGH + 2 * c

            def normalise_first():
                n0 = Norm(0)
                for part in range(2 * CB):
                    n0.stats(part)
                n0.channel_means()
                n0.group_out()
                n0.variance()
                for _ in range(3):
                    n0.newton()
                n0.factors()
                for c in range(CB):
                    n0.apply(c)
                assert n0.n == STAT

            dve.wait_ge(s_par_in, 64)
            dve.wait_ge(s_const, 7)
            for n in range(WT_TILES + 3):
                if n == 2:
                    normalise_first()
                if n == 9:
                    spread_v()
                if n == 12:
                    dve.wait_ge(s_rowb, 1)
                if n < WT_TILES:
                    product(n)
                if 1 <= n <= WT_TILES:
                    guard(n - 1)
                if n < WT_TILES:
                    dot(n)
                if 1 <= n <= WT_TILES:
                    power(n - 1)
                if n >= 3:
                    low_weights(n - 3)
                if 1 <= n <= WT_TILES:
                    inverse(n - 1)
                    undo(n - 1)

            def row_max(K, buf):
                dve.wait_ge(s_scores, K + 1)
                dve.tensor_reduce(nmax[:, buf:buf + 1], scores[:, buf, :], AX.X, ALU.max,
                                  negate=True).then_inc(s_max, 1)

            def low(K, buf, head, tt, half, ubuf):
                dve.wait_ge(s_phi, 2 * K + half + 1)
                at = (slice(None), ubuf, head, slice(4 * half, 4 * half + 4), slice(tt * P, (tt + 1) * P))
                dve.scalar_tensor_tensor(out=pt_lo[at], in0=tr[:, half], scalar=P_SCALE, in1=pt_hi[at],
                                         op0=ALU.mult, op1=ALU.subtract).then_inc(s_plo, 1)

            def reciprocals(unit, ubuf, again):
                dve.wait_ge(s_exp, 4 * unit + 4)
                if again:
                    dve.wait_ge(s_rt, unit)
                dve.reciprocal(rcp, sums[:, ubuf, :]).then_inc(s_rcp, 1)
                dve.wait_ge(s_rcp, unit + 1)
                for head in range(2):
                    for tt in range(2):
                        col = rcp[:, 2 * head + tt:2 * head + tt + 1]
                        ins = dve.tensor_scalar(rb[:, tt, head, :], ident[:, 0:HD], 0.0, col, ALU.mult, ALU.add)
                ins.then_inc(s_rb, 1)

            def normalise(unit, again):
                dve.wait_ge(s_rt, unit + 1)
                if again:
                    dve.wait_ge(s_on, unit)
                dve.tensor_copy(onorm[:], acc[:, 1, :]).then_inc(s_rs, 1)
                dve.wait_ge(s_rs, unit + 1)
                dve.scalar_tensor_tensor(out=onorm[:], in0=acc[:, 0, :], scalar=1.0 / P_SCALE, in1=onorm[:],
                                         op0=ALU.mult, op1=ALU.mult).then_inc(s_norm, 1)

            row_max(0, 0)
            row_max(1, 1)

            def batch(b):
                first, last = isinstance(b, int) and b == 0, isinstance(b, int) and b == B - 1
                norm = None if last else Norm(b + 1)
                for k in range(STEPS):
                    K, u, i = STEPS * b + k, k // 4, k % 4
                    if not (last and k >= STEPS - 2):
                        row_max(K + 2, k % 2)
                    if norm and k == 36:
                        norm.group_out()
                    for half in range(2):
                        low(K, k % 2, i // 2, i % 2, half, u % 2)
                    if i == 0 and not (first and u == 0):
                        reciprocals(UNITS * b + u - 1, (u - 1) % 2, not (first and u == 1))
                    if i == 3 and not (first and u == 0):
                        normalise(UNITS * b + u - 1, not (first and u == 1))
                    if norm:
                        if 20 <= k < 28:
                            norm.stats(k - 20)
                        if k == 32:
                            norm.channel_means()
                        if k == 36:
                            norm.variance()
                        if 37 <= k < 40:
                            norm.newton()
                        if k == 39:
                            norm.factors()
                        if 40 <= k < 44:
                            if k == 40:
                                dve.wait_ge(s_chunk, number(b, 19) + 1)
                            norm.apply(k - 40)
                if norm:
                    assert norm.n == STAT

            batch(0)
            with dve.Fori(1, B - 1) as b:
                batch(b)
            batch(B - 1)
            end = UNITS * B
            reciprocals(end - 1, 1, True)
            normalise(end - 1, True)

        @block.sync
        def _(sp):
            def stack(pairno, par, j, high_part, low_part, number_):
                which, h = KINDS[j]
                sp.wait_ge(s_split, number_ + 1)
                cols = slice(h * HALF, (h + 1) * HALF)
                for head in range(2):
                    rows = slice(head * HD, (head + 1) * HD)
                    high, low = high_part[rows], low_part[rows]
                    if which == "k":
                        moves = [(k_hi[r, par, head, cols], high) for r in (slice(0, HD), slice(HD, P))]
                        moves += [(k_lo[r, par, head, cols], low) for r in (slice(0, HD), slice(HD, P))]
                    elif h == 0:
                        moves = [(q0[0:HD, head, :], high), (q0[HD:P, head, :], low)]
                    else:
                        moves = [(q1[0:HD, par, head, :], high), (q1[HD:P, par, head, :], low)]
                    for dst, src in moves:
                        sp.dma_start(dst.bitcast(F32), src).then_inc(s_stk[j % 2], 16)

            def load_x(b):
                hold(sp)
                sp.dma_start(xs[:], xv[b]).then_inc(s_x_in, 16)

            def chunk_view(dram, b, r8):
                ot, h = r8 % 4, r8 // 4
                return dram[b, :, ot, h * HALF:(h + 1) * HALF]

            def buf(r8):
                return hs[:, r8 % 2, :]

            def load_residual(b, r8):
                hold(sp)
                sp.dma_start(buf(r8), chunk_view(xv, b, r8)).then_inc(s_res[r8 % 2], 16)

            def store(b, r8):
                hold(sp)
                sp.dma_start(chunk_view(ov, b, r8), buf(r8)).then_inc(s_out[r8 % 2], 16)

            sp.dma_start(gamma_row, gamma.rearrange("(o c) -> o c", o=1).broadcast_to([P, C])).then_inc(s_par_in, 16)
            sp.dma_start(beta_row, beta.rearrange("(o c) -> o c", o=1).broadcast_to([P, C])).then_inc(s_par_in, 16)
            sp.dma_start(bias[:, 0:12], qkv_b.rearrange("(t p) -> p t", p=P), allow_slow_non_contiguous=True).then_inc(s_par_in, 16)
            sp.dma_start(bias[:, 12:16], proj_b.rearrange("(t p) -> p t", p=P), allow_slow_non_contiguous=True).then_inc(s_par_in, 16)
            STACK_AFTER = (9, 12, 14, 15)
            for n in range(WT_TILES):
                if n == 2:
                    load_x(0)
                if n >= WRING:
                    sp.wait_ge(s_setup, setup_at["dot", n - WRING])
                t = ORDER[n]
                src = qkv_w[t * P:(t + 1) * P, :] if t < 12 else proj_w[(t - 12) * P:(t - 11) * P, :]
                sp.dma_start(raw_weights[n % WRING], src).then_inc(s_w_in[n % WRING], 16)
                if n in STACK_AFTER:
                    j = STACK_AFTER.index(n)
                    stack(0, 0, j, pre_hs[j], pre_fl[j], j)

            def batch(b):
                first, last = isinstance(b, int) and b == 0, isinstance(b, int) and b == B - 1
                if not last:
                    sp.wait_ge(s_xlo, CB * (b + 1))
                    load_x(b + 1)
                for m in range(NCH):
                    kind, db, what = slot(b, m)
                    if not active(b, m):
                        continue
                    c = number(b, m)
                    if kind == QK:
                        pairno = (b + db) * PAIRS + what[0]
                        j = what[1]
                        if not (first and what[0] == 1 and db == 0 and j != 3):
                            sp.wait_ge(s_scores, 16 * (pairno - 1) + (8 if j == 3 else 0))
                            hold(sp)
                        stack(pairno, what[0] % 2, j, hs[:, j % 2, :], fl[:, m % 2, :], c)
                        if j == 3 and 0 < m // 8 < 3 and not first:
                            for r in range(2):
                                sp.wait_ge(s_stk[r], stacked(pairno, 2 + r))
                                load_residual(b - 1, (m // 8 - 1) * 4 + r)
                    if kind == PROJ:
                        sp.wait_ge(s_split, c + 1)
                        store(b - 1, what)
                        if what % 4 < 2:
                            sp.wait_ge(s_out[what % 2], 16 * (4 * (b - 1) + what // 2 + 1))
                            load_residual(b - 1, what + 2)

            batch(0)
            with sp.Fori(1, B - 1) as b:
                batch(b)
            batch(B - 1)
            for r in range(8):
                if r == 0:
                    load_residual(B - 1, 0)
                    load_residual(B - 1, 1)
                sp.wait_ge(s_split, NCH * (B - 1) + 24 + r + 1)
                store(B - 1, r)
                if r < 6:
                    sp.wait_ge(s_out[r % 2], 16 * (4 * (B - 1) + r // 2 + 1))
                    load_residual(B - 1, r + 2)
            for r in range(2):
                sp.wait_ge(s_out[r], 16 * 4 * B)

        @block.gpsimd
        def _(pool):
            pool.memset(ident[:], 0.0).then_inc(s_const, 1)
            pool.memset(grp[:], GROUPS / C).then_inc(s_const, 1)
            pool.memset(inv[:, WT_TILES:WT_TILES + 1], V_SCALE).then_inc(s_const, 1)
            pool.memset(bias[:, WT_TILES:WT_TILES + 1], 0.0).then_inc(s_const, 1)
            pool.wait_ge(s_const, 4)
            pool.affine_select(out=ident[:], in_=ident[:], compare_op=ALU.not_equal, fill=1.0, base=0,
                               pattern=[[-1, P]], channel_multiplier=1).then_inc(s_const, 1)
            g3 = grp[:].rearrange("p (g j) -> p g j", j=C // GROUPS)
            pool.affine_select(out=g3, in_=g3, compare_op=ALU.is_ge, fill=0.0, base=0,
                               pattern=[[-(C // GROUPS), P * GROUPS // C], [0, C // GROUPS]],
                               channel_multiplier=1).then_inc(s_const, 1)
            pool.wait_ge(s_const, 6)
            pool.affine_select(out=g3, in_=g3, compare_op=ALU.is_ge, fill=0.0, base=C // GROUPS - 1,
                               pattern=[[C // GROUPS, P * GROUPS // C], [0, C // GROUPS]],
                               channel_multiplier=-1).then_inc(s_const, 1)

            def x_low(b, c):
                pool.wait_ge(s_stat, STAT * b + X_HIGH + 2 * c)
                pool.tensor_tensor(xn_lo[:, c, :], xs[:, c, :], xn_hi[:, c, :], ALU.subtract).then_inc(s_xlo, 1)

            def split(b, kind, what, c, flat, high, n, vno, proj_r):
                pool.wait_ge(s_ev, c + 1)
                hold(pool)
                if kind == QK:
                    j = what[1]
                    pool.tensor_copy(high.bitcast(F32R), flat).then_inc(s_qkh, 1)
                    pool.wait_ge(s_qkh, n + 1)
                    pool.tensor_tensor(flat.bitcast(F32R), flat, high,
                                       ALU.subtract).then_inc(s_split, 1)
                elif kind == V:
                    g, j = what
                    dst = [v[:, 2 * j:2 * j + 2, g * 256:(g + 1) * 256] for v in (v_hi, v_lo)]
                    src = flat.rearrange("p (s d) -> p s d", s=2)
                    pool.tensor_copy(dst[0], src).then_inc(s_vh, 1)
                    pool.wait_ge(s_vh, vno + 1)
                    pool.tensor_tensor(dst[1], src, dst[0], ALU.subtract).then_inc(s_split, 1)
                else:
                    r = what
                    pool.wait_ge(s_res[r % 2], 16 * (proj_r * 4 + r // 2 + 1))
                    pool.tensor_tensor(high, flat, high, ALU.add).then_inc(s_split, 1)

            def out_split(unit, par, u):
                p, q = divmod(u, 4)
                pool.wait_ge(s_norm, unit + 1)
                hold(pool)
                at = bass.ds(par * (CB * T) + (p * T + q * QT), QT)
                pool.tensor_copy(on_hi[:, at], onorm[:]).then_inc(s_onh, 1)
                pool.wait_ge(s_onh, unit + 1)
                pool.tensor_tensor(on_lo[:, at], onorm[:], on_hi[:, at], ALU.subtract).then_inc(s_on, 1)

            for c in range(CB):
                x_low(0, c)
            for c, (kind, what) in enumerate(PRE_CHUNKS):
                split(0, kind, what, c, pre_fl[c], pre_hs[c] if kind == QK else None, c, c - 4, 0)

            def batch(b):
                first, last = isinstance(b, int) and b == 0, isinstance(b, int) and b == B - 1
                for k in range(STEPS):
                    if k % 2 == 0:
                        m = k // 2 - 1 if k else NCH - 1
                        if k and active(b, m):
                            kind, db, what = slot(b, m)
                            if kind == QK:
                                pairno, j = (b + db) * PAIRS + what[0], what[1]
                                if j >= 2:
                                    pool.wait_ge(s_stk[j % 2], stacked(pairno, j - 2))
                                elif m // 8 < 2 or first:
                                    pool.wait_ge(s_stk[j % 2], stacked(pairno - 1, 2 + j))
                                else:
                                    pool.wait_ge(s_out[j % 2], 16 * (4 * (b - 1) + 2 * (m // 8 - 1)))
                                split(b, kind, what, number(b, m), fl[:, m % 2, :], hs[:, j % 2, :],
                                      qk_number(b, m), 0, 0)
                            elif kind == V:
                                if what[1] == 0 and not (first and db == 0):
                                    pool.wait_ge(s_pv, UNITS * b + (8 if db else 0))
                                split(b, kind, what, number(b, m), fl[:, m % 2, :], None, 0, v_number(b, m), 0)
                            else:
                                split(b, kind, what, number(b, m), fl[:, m % 2, :], hs[:, what % 2, :], 0, 0, b - 1)
                        if k == 0 and not first:
                            split(b, V, (0, 3), NCH * b - 1, fl[:, 1, :], None, 0, b * 8 + 3, 0)
                    if k % 4 == 0:
                        u = k // 4
                        if u >= 2:
                            out_split(UNITS * b + u - 2, parity(b), u - 2)
                        elif not first:
                            out_split(UNITS * b + u - 2, parity(b + 1), UNITS + u - 2)
                    if not last and 41 <= k < 41 + CB:
                        x_low(b + 1, k - 41)

            batch(0)
            with pool.Fori(1, B - 1) as b:
                batch(b)
            batch(B - 1)
            for u in (UNITS - 2, UNITS - 1):
                out_split(UNITS * (B - 1) + u, parity(B - 1), u)
            for r in range(8):
                split(B - 1, PROJ, r, NCH * (B - 1) + 24 + r, fl[:, r % 2, :], hs[:, r % 2, :], 0, 0, B - 1)

        @block.scalar
        def _(act):
            def evacuate(c, flat, kind, what, bank=None):
                act.wait_ge(s_chunk, c + 1)
                t = tiles_of(kind, what)
                act.activation(flat, mix[:] if bank is None else bank, ACT.Identity, scale=inv[:, t:t + 1],
                               bias=bias[:, t:t + 1]).then_inc(s_ev, 1)

            def exp(K, buf, again, ubuf, i, unit):
                act.wait_ge(s_max, K + 1)
                if again:
                    act.wait_ge(s_rcp, unit - 1)
                act.activation(prob[:, buf, :], scores[:, buf, :], ACT.Exp, bias=nmax[:, buf:buf + 1], scale=1.0,
                               accum_out=sums[:, ubuf, i:i + 1]).then_inc(s_exp, 1)

            def high(K, head, tt, half, ubuf):
                act.wait_ge(s_tr, 2 * K + half + 1)
                dst = pt_hi[:, ubuf, head, 4 * half:4 * half + 4, tt * P:(tt + 1) * P]
                act.activation(dst, tr[:, half], ACT.Copy, scale=P_SCALE).then_inc(s_phi, 1)

            act.wait_ge(s_const, 7)
            for n in range(WT_TILES + 2):
                if n < WT_TILES:
                    t = ORDER[n]
                    act.wait_ge(s_setup, setup_at["product", n])
                    if n:
                        act.wait_ge(s_wsum, n)
                    act.activation(junk_act, scaled_weights[n % WRING], ACT.Abs,
                                   accum_out=tot[:, t:t + 1]).then_inc(s_wsum, 1)
                if 1 <= n <= WT_TILES:
                    t = ORDER[n - 1]
                    act.wait_ge(s_setup, setup_at["inverse", n - 1])
                    w = scaled_weights[(n - 1) % WRING]
                    act.activation(w, w, ACT.Copy, scale=rc[:, t:t + 1]).then_inc(s_wsc, 1)
                if n - 2 in FIRST_AFTER:
                    c = FIRST_AFTER.index(n - 2)
                    kind, what = PRE_CHUNKS[c]
                    if c % 2 == 0 and c < 4:
                        act.wait_ge(s_setup, setup_at["undo", c // 2])
                    evacuate(c, pre_fl[c], kind, what, pre_bank[c % 2])
                if n >= 2:
                    t = ORDER[n - 2]
                    act.wait_ge(s_wtr, n - 1)
                    act.activation(wt_hi[:, :, t * P:(t + 1) * P], weight_bank(n - 2), ACT.Copy,
                                   scale=W_TOP).then_inc(s_wh, 1)
            exp(0, 0, False, 0, 0, 0)
            act.wait_ge(s_split, PRE)
            exp(1, 1, False, 0, 1, 0)

            def batch(b):
                first, last = isinstance(b, int) and b == 0, isinstance(b, int) and b == B - 1
                for k in range(STEPS):
                    K, u, i = STEPS * b + k, k // 4, k % 4
                    if k == 0 and not first:
                        act.wait_ge(s_split, NCH * b - 2)
                        evacuate(NCH * b - 1, fl[:, 1, :], V, (0, 3))
                    if k and k % 2 == 0 and active(b, k // 2 - 1):
                        m = k // 2 - 1
                        kind, db, what = slot(b, m)
                        c = number(b, m)
                        before = m - 2
                        while before >= 0 and not active(b, before):
                            before -= 2
                        if before >= 0 and slot(b, before)[0] == QK:
                            _, pdb, (pp, pj) = slot(b, before)
                            act.wait_ge(s_stk[pj % 2], stacked((b + pdb) * PAIRS + pp, pj))
                        else:
                            act.wait_ge(s_split, c - 1)
                        evacuate(c, fl[:, m % 2, :], kind, what)
                    if i == 0 and not (first and u < 2):
                        act.wait_ge(s_pv, UNITS * b + u - 1)
                    for half in range(2):
                        high(K, i // 2, i % 2, half, u % 2)
                    if not (last and k >= STEPS - 2):
                        u2, i2 = divmod(k + 2, 4)
                        exp(K + 2, k % 2, i2 == 0 and not (first and u2 < 2), u2 % 2, i2, UNITS * b + u2)

            batch(0)
            with act.Fori(1, B - 1) as b:
                batch(b)
            batch(B - 1)
            for r in range(8):
                c = NCH * (B - 1) + 24 + r
                act.wait_ge(s_split, c - 1)
                evacuate(c, fl[:, r % 2, :], PROJ, r)

        @block.tensor
        def _(pe):
            pe.wait_ge(s_const, 7)

            def transpose_weights(n):
                if n == 9:
                    pe.wait_ge(s_setup, setup_at["spread"])
                    for i in range(4):
                        pe.transpose(v_scale_row[:, i * P:(i + 1) * P], prob[:, 0, i * P:(i + 1) * P], ident[:])
                    for i in range(4):
                        last_t = pe.transpose(v_bias_row[:, i * P:(i + 1) * P], prob[:, 0, (4 + i) * P:(5 + i) * P],
                                              ident[:])
                    last_t.then_inc(s_rowb, 1)
                pe.wait_ge(s_wsc, n + 1)
                if n >= 4:
                    pe.wait_ge(s_wl, n - 3)
                for c in range(CB):
                    tp = pe.transpose(weight_bank(n)[:, c], scaled_weights[n % WRING][:, c * P:(c + 1) * P], ident[:])
                tp.then_inc(s_wtr, 1)

            TERMS = [("h", "h"), ("h", "l"), ("l", "h")]
            WTT = {"h": wt_hi, "l": wt_lo}
            XN = {"h": xn_hi, "l": xn_lo}
            ON = {"h": on_hi, "l": on_lo}

            def chunk_half(kind, what, half, par=0, bank=None):
                bank = mix[:] if bank is None else bank
                if kind == V:
                    g, j = what
                    s = 2 * j + half
                    for n, (a, w) in enumerate(TERMS):
                        for c in range(CB):
                            mm = pe.matmul(bank[:, half * 256:(half + 1) * 256], XN[a][:, c, s * P:(s + 1) * P],
                                           WTT[w][:, c, 2 * C + g * 256:2 * C + (g + 1) * 256],
                                           start=(n == 0 and c == 0), stop=(n == 2 and c == CB - 1))
                    return mm
                t = tiles_of(kind, what)
                h = KINDS[what[1]][1] if kind == QK else what // 4
                for e in range(6 * half, 6 * half + 6):
                    (w, a), c = TERMS[e // CB], e % CB
                    if kind == QK:
                        rhs = XN[a][:, c, h * HALF:(h + 1) * HALF]
                    else:
                        rhs = ON[a][:, bass.ds(par * (CB * T) + (c * T + h * HALF), HALF)]
                    mm = pe.matmul(bank, WTT[w][:, c, t * P:(t + 1) * P], rhs, start=(e == 0), stop=(e == 11))
                return mm

            def group_sums(b):
                pe.wait_ge(s_stat, STAT * b + GROUP_IN)
                pe.matmul(acc[:, 1, 0:8], grp[:], xstat[:, 56:64], start=True, stop=True).then_inc(s_gsum, 1)

            def step_scores(k, buf):
                p, s = divmod(k % STEPS, 16)
                tile_, head = 2 * (s // 4) + s % 2, (s % 4) // 2
                lhs = q0[:, head, tile_ * P:(tile_ + 1) * P] if tile_ < 4 else \
                    q1[:, p % 2, head, (tile_ - 4) * P:(tile_ - 3) * P]
                for sh in range(2):
                    cols = slice(sh * HALF, (sh + 1) * HALF)
                    for n, kk in enumerate((k_hi, k_lo)):
                        mm = pe.matmul(scores[:, buf, cols], lhs, kk[:, p % 2, head, cols],
                                       start=(n == 0), stop=(n == 1))
                mm.then_inc(s_scores, 1)

            def pair_ready(pairno):
                for r in range(2):
                    pe.wait_ge(s_stk[r], 192 * (pairno + 1))

            def step_transposes(K, buf, waits):
                for half in range(2):
                    if waits:
                        pe.wait_ge(s_plo, 2 * K - 1 + half)
                    for j in range(4):
                        s = 4 * half + j
                        tp = pe.transpose(tr[:, half, j, :], prob[:, buf, s * P:(s + 1) * P], ident[:])
                    tp.then_inc(s_tr, 1)

            def prob_v(ubuf, u, i):
                for s in (2 * i, 2 * i + 1):
                    for n, (pt, v) in enumerate(((pt_hi, v_hi), (pt_lo, v_hi), (pt_hi, v_lo))):
                        for head in range(2):
                            d = (2 * (u // 4) + head) * HD
                            mm = pe.matmul(acc[head * HD:(head + 1) * HD, 0, :], v[:, s, d:d + HD],
                                           pt[:, ubuf, head, s, :], start=(s == 0 and n == 0),
                                           stop=(s == ST - 1 and n == 2))
                return mm

            def unit_sums(unit):
                pe.wait_ge(s_rb, unit + 1)
                for tt in range(2):
                    tp = pe.transpose(acc[:, 1, tt * P:(tt + 1) * P], rb[:, tt].rearrange("p a b -> p (a b)"), ident[:])
                tp.then_inc(s_rt, 1)

            transpose_weights(0)
            group_sums(0)
            pe.wait_ge(s_stat, GROUP_OUT)
            transpose_weights(1)
            transpose_weights(2)
            pe.wait_ge(s_xlo, CB)
            for c, (kind, what) in enumerate(PRE_CHUNKS):
                pe.wait_ge(s_wl, (1, 1, 2, 2, 4, 4, 4, 4)[c])
                if c >= 2:
                    pe.wait_ge(s_ev, c - 1)
                chunk_half(kind, what, 0, bank=pre_bank[c % 2])
                chunk_half(kind, what, 1, bank=pre_bank[c % 2]).then_inc(s_chunk, 1)
                for n in range(FIRST_AFTER[c], FIRST_AFTER[c] + TILES_AFTER[c]):
                    transpose_weights(n)
            pe.wait_ge(s_wl, WT_TILES)
            pe.wait_ge(s_ev, PRE)
            pair_ready(0)
            step_scores(0, 0)
            step_scores(1, 1)

            def batch(b):
                first, last = isinstance(b, int) and b == 0, isinstance(b, int) and b == B - 1
                for k in range(STEPS):
                    K, u, i, m = STEPS * b + k, k // 4, k % 4, k // 2

                    def chunk():
                        if not active(b, m):
                            return
                        kind, db, what = slot(b, m)
                        c = number(b, m)
                        if k % 2 == 0:
                            pe.wait_ge(s_ev, c)
                            if kind == QK and m == 24:
                                pe.wait_ge(s_xlo, CB * (b + 2))
                            if kind == PROJ:
                                pe.wait_ge(s_on, UNITS * b)
                        mm = chunk_half(kind, what, k % 2, parity(b + 1))
                        if k % 2:
                            mm.then_inc(s_chunk, 1)

                    def values():
                        if first and u == 0:
                            return
                        if i == 0:
                            if not (first and u == 1):
                                pe.wait_ge(s_norm, UNITS * b + u - 1)
                            if k == 36 and not last:
                                pe.wait_ge(s_stat, STAT * (b + 1) + GROUP_OUT)
                            pe.wait_ge(s_plo, 2 * K)
                            if u == 1:
                                pe.wait_ge(s_split, PRE if first else NCH * b)
                            if u == 9:
                                pe.wait_ge(s_split, number(b, 7) + 1)
                        mm = prob_v((u - 1) % 2, (u - 1) % UNITS, i)
                        if i == 3:
                            mm.then_inc(s_pv, 1)
                            unit_sums(UNITS * b + u - 1)

                    if k % 2:
                        values()
                    pe.wait_ge(s_exp, K + 1)
                    if not (last and k >= STEPS - 2):
                        if (k + 2) % 16 == 0:
                            pair_ready(PAIRS * b + (k + 2) // 16)
                        step_scores(k + 2, k % 2)
                    step_transposes(K, k % 2, not (first and k == 0))
                    if k == 36 and not last:
                        pe.wait_ge(s_norm, UNITS * b + u - 1)
                        group_sums(b + 1)
                    chunk()
                    if k % 2 == 0:
                        values()

            batch(0)
            with pe.Fori(1, B - 1) as b:
                batch(b)
            batch(B - 1)
            end = UNITS * B
            pe.wait_ge(s_norm, end - 1)
            pe.wait_ge(s_plo, 8 * end)
            for i in range(4):
                mm = prob_v(1, UNITS - 1, i)
            mm.then_inc(s_pv, 1)
            unit_sums(end - 1)
            pe.wait_ge(s_on, end)
            for r in range(8):
                pe.wait_ge(s_ev, NCH * (B - 1) + 24 + r)
                chunk_half(PROJ, r, 0, parity(B - 1))
                chunk_half(PROJ, r, 1, parity(B - 1)).then_inc(s_chunk, 1)


def kernel(**inputs):
    import numpy as np
    import concourse.bacc as bacc
    from concourse import mybir as mb
    from concourse.bass_utils import run_bass_kernel_spmd as run

    names = ["x", "L0_conv_gn_gamma", "L0_conv_gn_beta", "L0_conv_qkv_w", "L0_conv_qkv_b", "L0_conv_proj_w",
             "L0_conv_proj_b"]
    nc = bacc.Bacc("TRN2", target_bir_lowering=False, num_devices=1)
    arrays, args = {}, []
    for name in names:
        a = np.ascontiguousarray(inputs[name])
        arrays[f"in_{name}"] = a
        args.append(nc.dram_tensor(f"in_{name}", a.shape, mb.dt.from_np(a.dtype), kind="ExternalInput").ap())
    shape = np.shape(inputs["x"])
    args.append(nc.dram_tensor("out_0", shape, mb.dt.float32, kind="ExternalOutput").ap())
    attention_block(nc, *args)
    r = run(nc, [arrays], core_ids=[0])
    return r.results[0]["out_0"]
```
